# Optimizing a Trainium2 kernel written in Bass

```python
import numpy as np
import jax
import jax.numpy as jnp

def _softmax(x, axis=-1):
    return jax.nn.softmax(x, axis=axis)

def _gelu(x):
    return jax.nn.gelu(x, approximate=True)

def _silu(x):
    return jax.nn.silu(x)

def _sigmoid(x):
    return jax.nn.sigmoid(x)

def _layernorm(x, axis=-1, eps=1e-05):
    m = jnp.mean(x, axis=axis, keepdims=True)
    v = jnp.var(x, axis=axis, keepdims=True)
    return (x - m) / jnp.sqrt(v + eps)

def _scatter_add(tgt, idx, src, axis=0):
    return tgt.at[idx].add(src)

def _segment_sum(src, seg, n):
    return jax.ops.segment_sum(src, seg, n)
kernel_name = 'mk_cond_resid_d2_seqx_r2_b55d95'

def setup_inputs(seed: int=0):
    np.random.seed(seed)
    _w = jnp.asarray

    def _rec_inputs():
        import jax
        import jax.numpy as jnp
        _rk = jax.random.key(seed)
        x = -7.109e-05 + 0.9999 * jax.random.normal(jax.random.fold_in(_rk, 1), (8, 512, 2048), jnp.float32)
        _lenS = 512 - jax.random.randint(jax.random.fold_in(_rk, 7), (8,), 0, max(1, 512 // 4) + 1, jnp.int32)
        _lenS2 = 512 - jax.random.randint(jax.random.fold_in(_rk, 8), (8,), 0, max(1, 512 // 4) + 1, jnp.int32)
        itok_B_4_50 = jax.random.randint(jax.random.fold_in(_rk, 11), (8,), 4, 51, jnp.int32)
        itok_B_1_7 = jax.random.randint(jax.random.fold_in(_rk, 12), (8,), 1, 8, jnp.int32)
        return (x, itok_B_4_50, itok_B_1_7)
    x, itok_B_4_50, itok_B_1_7 = _rec_inputs()

    def _L0_cond_setup():
        import jax, jax.numpy as jnp
        import numpy as np
        RANK = 16
        ALPHA = 16.0
        SCALING = ALPHA / RANK
        key = jax.random.key(seed)
        k1, k2, k3, k4 = jax.random.split(key, 4)
        batch, n_tok, d_in, d_out, n_adapters, rank = (8, 1024, 2048, 2048, 64, RANK)
        x = jax.random.normal(k1, (batch, n_tok, d_in), dtype=jnp.float32)
        A = jax.random.normal(k2, (n_adapters, d_out, rank), dtype=jnp.float32) * 0.02
        B = jax.random.normal(k3, (n_adapters, rank, d_in), dtype=jnp.float32)
        adapter_ids = jax.random.randint(k4, (batch,), 0, n_adapters, dtype=jnp.int32)
        return {'x': x, 'A': A, 'B': B, 'adapter_ids': adapter_ids}
    _L0_cond_all = _L0_cond_setup()
    _L0_cond_in = {k: v for k, v in _L0_cond_all.items() if k in ('A', 'B')}
    del _L0_cond_all

    def _L1_cond_setup():
        import jax, jax.numpy as jnp
        import numpy as np
        B, S, D_IN, D_OUT = (4, 1024, 2048, 2048)
        N_ADAPTERS, MAX_RANK = (8, 16)
        key = jax.random.key(seed)
        ks = jax.random.split(key, 7)
        x = jax.random.normal(ks[0], (B, S, D_IN), dtype=jnp.float32)
        weight = jax.random.normal(ks[1], (D_OUT, D_IN), dtype=jnp.float32) * (1.0 / np.sqrt(D_IN))
        bias = jax.random.normal(ks[2], (D_OUT,), dtype=jnp.float32) * 0.01
        lora_a_weights = jax.random.normal(ks[3], (N_ADAPTERS, MAX_RANK, D_IN), dtype=jnp.float32) * (1.0 / np.sqrt(D_IN))
        lora_b_weights = jax.random.normal(ks[4], (N_ADAPTERS, D_OUT, MAX_RANK), dtype=jnp.float32) * 0.02
        scaling_factors = jax.random.uniform(ks[5], (N_ADAPTERS,), dtype=jnp.float32, minval=0.5, maxval=2.0)
        adapter_id = jax.random.randint(ks[6], (B,), 0, N_ADAPTERS, dtype=jnp.int64)
        return {'x': x, 'weight': weight, 'bias': bias, 'lora_a_weights': lora_a_weights, 'lora_b_weights': lora_b_weights, 'scaling_factors': scaling_factors, 'adapter_id': adapter_id}
    _L1_cond_all = _L1_cond_setup()
    _L1_cond_in = {k: v for k, v in _L1_cond_all.items() if k in ('weight', 'bias', 'lora_a_weights', 'lora_b_weights', 'scaling_factors')}
    del _L1_cond_all
    return {'x': x, 'itok_B_4_50': itok_B_4_50, 'itok_B_1_7': itok_B_1_7, 'L0_cond_A': _L0_cond_in['A'], 'L0_cond_B': _L0_cond_in['B'], 'L1_cond_weight': _L1_cond_in['weight'], 'L1_cond_bias': _L1_cond_in['bias'], 'L1_cond_lora_a_weights': _L1_cond_in['lora_a_weights'], 'L1_cond_lora_b_weights': _L1_cond_in['lora_b_weights'], 'L1_cond_scaling_factors': _L1_cond_in['scaling_factors']}

def reference(x, itok_B_4_50, itok_B_1_7, L0_cond_A, L0_cond_B, L1_cond_weight, L1_cond_bias, L1_cond_lora_a_weights, L1_cond_lora_b_weights, L1_cond_scaling_factors):
    import jax
    import jax.numpy as jnp

    def _L0_cond_ref(x, A, B, adapter_ids):
        import jax, jax.numpy as jnp
        import numpy as np
        RANK = 16
        ALPHA = 16.0
        SCALING = ALPHA / RANK
        B_req = B[adapter_ids]
        A_req = A[adapter_ids]
        Bx = jnp.einsum('bni,bri->bnr', x, B_req)
        out = jnp.einsum('bnr,bor->bno', Bx, A_req)
        return out * SCALING

    def _L1_cond_ref(x, weight, bias, lora_a_weights, lora_b_weights, scaling_factors, adapter_id):
        import jax, jax.numpy as jnp
        import numpy as np
        B, S, D_IN, D_OUT = (4, 1024, 2048, 2048)
        N_ADAPTERS, MAX_RANK = (8, 16)
        base = jnp.einsum('bsi,oi->bso', x, weight) + bias
        a_sel = lora_a_weights[adapter_id]
        b_sel = lora_b_weights[adapter_id]
        scale = scaling_factors[adapter_id]
        low = jnp.einsum('bsi,bri->bsr', x, a_sel)
        delta = jnp.einsum('bsr,bor->bso', low, b_sel)
        return base + scale[:, None, None] * delta
    x = x + _L0_cond_ref(x, L0_cond_A, L0_cond_B, itok_B_4_50)
    x = x + _L1_cond_ref(x, L1_cond_weight, L1_cond_bias, L1_cond_lora_a_weights, L1_cond_lora_b_weights, L1_cond_scaling_factors, itok_B_1_7)
    return x

_drawn_inputs = setup_inputs


def setup_inputs(seed=0):
    import zlib

    import numpy as np

    out = dict(_drawn_inputs(seed))
    spreads = {}
    factors = {'L1_cond_bias': 30.83, 'L1_cond_scaling_factors': 2.929}
    for name, (base, spread) in spreads.items():
        noise = np.random.default_rng([zlib.crc32(name.encode()), seed]).standard_normal(out[name].shape)
        drawn = base * np.exp(spread * noise) if base else spread * noise
        out[name] = jnp.asarray(drawn.astype(out[name].dtype))
    for name, factor in factors.items():
        out[name] = (out[name] * factor).astype(out[name].dtype)
    return out
```

```python
from contextlib import ExitStack

import concourse.bass as bass
from concourse import mybir

P = 128
ALU = mybir.AluOpType
ACT = mybir.ActivationFunctionType
F32 = mybir.dt.float32
F32R = mybir.dt.float32r
I32 = mybir.dt.int32

BATCH = 8
TOK = 512
DIM = 2048
RANK = 16
KC = DIM // P
PHASES = [range(0, 5), range(5, 10), range(10, 16)]
WIDEST = max(len(tiles) for tiles in PHASES)
XGROUP = 2
XGROUPS = KC // XGROUP
XRAW = 2
XSPLIT = 4
WRAW = 3
LAG = XSPLIT
G_HI, SB_HI, G_LO, SB_LO = range(4)
RANK_ROWS = [G_HI, SB_HI, G_LO, SB_LO, G_HI, SB_HI, G_HI, SB_HI]
N_ROW_DMAS = len(RANK_ROWS)


def two_adapter_layers(
    nc: bass.Bass,
    x_t: bass.AP,
    w_t: bass.AP,
    bias_t: bass.AP,
    A0_in: bass.AP,
    B0_in: bass.AP,
    a1_in: bass.AP,
    b1_in: bass.AP,
    scale_in: bass.AP,
    ids0: bass.AP,
    ids1: bass.AP,
    eye: bass.AP,
    same_batch: bass.AP,
    up_parts: bass.AP,
    out_t: bass.AP,
):
    n_adapters0, n_adapters1 = A0_in.shape[0], b1_in.shape[0]

    with ExitStack() as ctx:
        def sb(name, shape, dt=F32):
            return ctx.enter_context(nc.sbuf_tensor(name, shape, dt))

        def sem(name):
            return ctx.enter_context(nc.semaphore(name))

        w_hi = sb("w_hi", [P, KC, WIDEST * P], F32R)
        w_lo = sb("w_lo", [P, KC, WIDEST * P], F32R)
        w_raw = sb("w_raw", [P, WRAW, WIDEST * P])
        x_raw = sb("x_raw", [P, XRAW, XGROUP, TOK])
        x_hi = sb("x_hi", [P, XSPLIT, TOK], F32R)
        x_lo = sb("x_lo", [P, XSPLIT, TOK], F32R)
        z_rows = sb("z_rows", [P, BATCH, TOK], F32R)
        rank_w = sb("rank_w", [P, WIDEST * P], F32R)
        down_raw = sb("down_raw", [P, 2, KC, RANK])
        down = sb("down", [P, KC, P], F32R)
        A0_hi = sb("A0_hi", [P, KC, P], F32R)
        A0_lo = sb("A0_lo", [P, KC, P], F32R)
        up = sb("up", [P, 4, WIDEST * P], F32R)
        sb_raw = sb("sb_raw", [P, WIDEST * P])
        stage = sb("stage", [P, WIDEST, TOK])
        ident = sb("ident", [P, P])
        mask = sb("mask", [P, P])
        c_raw = sb("c_raw", [P, P])
        c_split = sb("c_split", [P, 2, P], F32R)
        bias_sb = sb("bias_sb", [P, KC])
        scale = sb("scale", [P, 1])
        ids = sb("ids", [1, 2, BATCH], I32)

        gathered = stage[:].rearrange("p t n -> p (t n)")[:, 0:BATCH * KC * RANK]
        gathered_bkr = gathered.rearrange("p (b k r) -> p k b r", b=BATCH, k=KC)
        z_flat = z_rows[:].rearrange("p b n -> p (b n)")
        a_hi = z_flat[:, 0:KC * P].rearrange("p (k m) -> p k m", k=KC)
        a_lo = z_flat[:, KC * P:2 * KC * P].rearrange("p (k m) -> p k m", k=KC)

        def as_bkr(t):
            return t.rearrange("p k (b r) -> p k b r", b=BATCH)

        banks = [ctx.enter_context(nc.psum_tensor(f"bank{i}", [P, TOK], F32)) for i in range(8)]
        z_bank = banks[5]
        g_banks = banks[6:8]
        c_bank = banks[0]

        ids_landed = sem("ids_landed")
        const_landed = sem("const_landed")
        A0_landed = sem("A0_landed")
        a_landed = sem("a_landed")
        b_landed = sem("b_landed")
        w_landed = [sem(f"w_landed{i}") for i in range(WRAW)]
        x_landed = [sem(f"x_landed{i}") for i in range(XRAW)]
        down_landed = sem("down_landed")
        parts_saved = sem("parts_saved")
        rank_w_landed = sem("rank_w_landed")
        stored = sem("stored")
        A0_rounded = sem("A0_rounded")
        A0_ready = sem("A0_ready")
        a_rounded = sem("a_rounded")
        a_ready = sem("a_ready")
        w_diag = sem("w_diag")
        w_rounded = sem("w_rounded")
        w_ready = sem("w_ready")
        x_rounded = sem("x_rounded")
        x_ready = sem("x_ready")
        down_rounded = sem("down_rounded")
        down_ready = sem("down_ready")
        chunk_done = sem("chunk_done")
        c_done = sem("c_done")
        c_masked = sem("c_masked")
        c_hi_done = sem("c_hi_done")
        c_ready = sem("c_ready")
        sb_hi_done = sem("sb_hi_done")
        sb_ready = sem("sb_ready")
        g_done = sem("g_done")
        g_hi_done = sem("g_hi_done")
        up_ready = sem("up_ready")
        z_done = sem("z_done")
        z_hi_done = sem("z_hi_done")
        z_ready = sem("z_ready")
        tile_done = sem("tile_done")
        evacuated = sem("evacuated")

        def tiles_before(ph):
            return BATCH * sum(len(t) for t in PHASES[:ph])

        block = ctx.enter_context(nc.Block())

        @block.sync
        def _(sp):
            def load_x(ph, b, g):
                n = (ph * BATCH + b) * KC + XGROUP * (g - XRAW)
                if not (ph == 0 and type(b) is int and b == 0 and g < XRAW):
                    sp.wait_ge(x_ready, n + XGROUP)
                sp.dma_start(x_raw[:, g % XRAW], x_t[bass.ds(b, 1), :, bass.ts(g, XGROUP), :]
                             .rearrange("b p k n -> (b p) k n")).then_inc(x_landed[g % XRAW], 16)

            def load_w(ph, k):
                tiles = PHASES[ph]
                n = ph * KC + k
                if n >= WRAW:
                    sp.wait_ge(w_ready, n - WRAW + 1)
                sp.dma_start(w_raw[:, n % WRAW, 0:len(tiles) * P],
                             w_t[k, :, tiles[0] * P:(tiles[-1] + 1) * P]
                             ).then_inc(w_landed[n % WRAW], 16)

            def adapter(layer, b):
                last = (n_adapters0, n_adapters1)[layer] - 1
                return sp.value_load(ids[0:1, layer, bass.ds(b, 1)], min_val=0, max_val=last)

            def load_down(b):
                sp.dma_start(down_raw[:, 0].rearrange("p k r -> p (k r)"),
                             B0_in[bass.ds(adapter(0, b), 1)].rearrange("a p m -> (a p) m")
                             ).then_inc(down_landed, 16)
                sp.dma_start(down_raw[:, 1].rearrange("p k r -> p (k r)"),
                             a1_in[bass.ds(adapter(1, b), 1)].rearrange("a p m -> (a p) m")
                             ).then_inc(down_landed, 16)

            def load_b(ph):
                tiles = PHASES[ph]
                if ph:
                    sp.wait_ge(sb_ready, ph)
                for b in range(BATCH):
                    sp.dma_start(sb_raw[b * RANK:(b + 1) * RANK, 0:len(tiles) * P],
                                 b1_in[bass.ds(adapter(1, b), 1), :, tiles[0] * P:(tiles[-1] + 1) * P]
                                 .rearrange("a r o -> (a r) o")).then_inc(b_landed, 16)

            def fill_rank_w(ph, b):
                width = len(PHASES[ph]) * P
                tiles = PHASES[ph]
                channels = slice(tiles[0] * P, (tiles[-1] + 1) * P)
                if type(b) is int and b == 0:
                    sp.wait_ge(up_ready, 2 * (ph + 1))
                    for part in range(4):
                        sp.dma_start(up_parts[part, :, channels],
                                     up[:, part, 0:width].bitcast(F32)).then_inc(parts_saved, 16)
                    sp.wait_ge(parts_saved, 16 * 4 * (ph + 1))
                if not (ph == 0 and type(b) is int and b == 0):
                    before = tiles_before(ph) + b * len(PHASES[ph])
                    sp.wait_ge(tile_done, before)
                for group, part in enumerate(RANK_ROWS):
                    sp.dma_start(rank_w[group * RANK:(group + 1) * RANK, 0:width].bitcast(F32),
                                 up_parts[part, bass.ds(b * RANK, RANK), channels]
                                 ).then_inc(rank_w_landed, 16)

            sp.dma_start(ids[:, 0], ids0).then_inc(ids_landed, 16)
            sp.dma_start(ids[:, 1], ids1).then_inc(ids_landed, 16)
            sp.dma_start(ident[:], eye).then_inc(const_landed, 16)
            load_w(0, 0)
            sp.wait_ge(ids_landed, 32)
            for b in range(BATCH):
                sp.dma_start(gathered[:, bass.ts(b, KC * RANK)],
                             A0_in[bass.ds(adapter(0, b), 1)].rearrange("a p m -> (a p) m")
                             ).then_inc(A0_landed, 16)
            for k in range(1, WRAW):
                load_w(0, k)
            sp.dma_start(mask[:], same_batch).then_inc(const_landed, 16)
            sp.dma_start(bias_sb[:], bias_t).then_inc(const_landed, 16)
            for b in range(BATCH):
                sp.dma_start(scale[bass.ts(b, RANK), :],
                             scale_in[bass.ds(adapter(1, b), 1)].rearrange("a r c -> (a r) c")
                             ).then_inc(const_landed, 16)
            sp.wait_ge(A0_ready, 1)
            for b in range(BATCH):
                sp.dma_start(gathered[:, bass.ts(b, KC * RANK)],
                             a1_in[bass.ds(adapter(1, b), 1)].rearrange("a p m -> (a p) m")
                             ).then_inc(a_landed, 16)
            load_b(0)
            load_down(0)
            for k in range(WRAW, KC):
                load_w(0, k)

            for ph in range(len(PHASES)):
                last_phase = ph == len(PHASES) - 1

                def load_batch(b, next_w=False, w_left=False):
                    for g in range(XGROUPS):
                        if next_w:
                            for k in range(max(0, XGROUP * g - 7), max(0, XGROUP * g - 5)):
                                load_w(ph + 1, k)
                        load_x(ph, b, g)
                        if g == LAG // XGROUP + 1 and ph == 0 and not (type(b) is int and b == BATCH - 1):
                            sp.wait_ge(down_ready, (b + 1) * KC)
                            load_down(b + 1)
                        if w_left and g == 1:
                            load_w(ph, KC - 1)
                        if g == XGROUPS // 2:
                            fill_rank_w(ph, b)
                            if next_w:
                                load_b(ph + 1)
                load_batch(0, w_left=ph > 0)
                with sp.Fori(1, BATCH if last_phase else BATCH - 1) as b:
                    load_batch(b)
                if not last_phase:
                    load_batch(BATCH - 1, next_w=True)
                    for k in range(KC - 7, KC - 1):
                        load_w(ph + 1, k)

        @block.scalar
        def _(act):
            def round_x(ph, b, j):
                n = (ph * BATCH + b) * KC + j
                g = j // XGROUP
                groups = (ph * BATCH + b) * (XGROUPS // XRAW) + g // XRAW + 1
                if j % XGROUP == 0:
                    act.wait_ge(x_landed[g % XRAW], 16 * groups)
                if not (ph == 0 and type(b) is int and b == 0 and j < LAG):
                    act.wait_ge(chunk_done, n - LAG + 1)
                nc.scalar.copy(x_hi[:, j % XSPLIT], x_raw[:, g % XRAW, j % XGROUP]
                               ).then_inc(x_rounded, 1)

            def round_w(ph, k):
                tiles = PHASES[ph]
                n, width = ph * KC + k, len(tiles) * P
                if ph:
                    act.wait_ge(chunk_done, (ph * BATCH - 1) * KC + k + 1)
                act.wait_ge(w_landed[n % WRAW], 16 * (n // WRAW + 1))
                if k in tiles:
                    act.wait_ge(w_diag, k + 1)
                nc.scalar.copy(w_hi[:, k, 0:width], w_raw[:, n % WRAW, 0:width]
                               ).then_inc(w_rounded, 1)

            def round_down(b, k):
                if k == 0:
                    act.wait_ge(down_landed, 32 * (b + 1))
                if not (type(b) is int and b == 0):
                    act.wait_ge(chunk_done, (b - 1) * KC + k + 1)
                nc.scalar.copy(down[:, k, 0:6 * RANK].rearrange("p (g s r) -> p g s r", g=3, s=2),
                               down_raw[:, :, k].unsqueeze(1).to_broadcast([P, 3, 2, RANK])
                               ).then_inc(down_rounded, 1)

            def results(ph, b):
                tiles = PHASES[ph]
                before = tiles_before(ph) + b * len(tiles)
                if not (ph == 0 and type(b) is int and b == 0):
                    act.wait_ge(stored, 16 * before)
                for t, tile in enumerate(tiles):
                    act.wait_ge(tile_done, before + t + 1)
                    nc.scalar.activation(stage[:, t], banks[t][:], ACT.Identity,
                                         bias=bias_sb[:, tile:tile + 1]).then_inc(evacuated, 1)
                for t, tile in enumerate(tiles):
                    act.wait_ge(evacuated, before + t + 1)
                    act.dma_start(out_t[bass.ds(b, 1), :, tile, :].rearrange("b p n -> (b p) n"),
                                  stage[:, t]).then_inc(stored, 16)

            def round_batch(ph, b, previous=None, next_w=False, w_left=False):
                for j in range(KC):
                    round_x(ph, b, j)
                    if w_left and j < LAG - 1:
                        round_w(ph, KC - LAG + j)
                    if j == LAG - 2 and previous is not None:
                        results(*previous)
                    if w_left and j == LAG - 1:
                        round_w(ph, KC - 1)
                    if next_w and j >= LAG:
                        round_w(ph + 1, j - LAG)
                    if ph == 0 and j < LAG and not (type(b) is int and b == 0):
                        round_down(b, KC - LAG + j)
                    if ph == 0 and j >= LAG and not (type(b) is int and b == BATCH - 1):
                        round_down(b + 1, j - LAG)

            act.wait_ge(A0_landed, 16 * BATCH)
            nc.scalar.copy(as_bkr(A0_hi[:]), gathered_bkr).then_inc(A0_rounded, 1)
            for k in range(KC // 2):
                round_w(0, k)
            act.wait_ge(a_landed, 16 * BATCH)
            nc.scalar.copy(as_bkr(a_hi), gathered_bkr).then_inc(a_rounded, 1)
            for k in range(KC // 2, KC):
                round_w(0, k)
            for k in range(KC):
                round_down(0, k)
            act.wait_ge(const_landed, 16 * (3 + BATCH))
            act.wait_ge(a_ready, 1)

            for ph in range(len(PHASES)):
                last_phase = ph == len(PHASES) - 1
                round_batch(ph, 0, (ph - 1, BATCH - 1) if ph else None, w_left=ph > 0)
                with act.Fori(1, BATCH if last_phase else BATCH - 1) as b:
                    round_batch(ph, b, (ph, b - 1))
                if not last_phase:
                    round_batch(ph, BATCH - 1, (ph, BATCH - 2), next_w=True)
            results(len(PHASES) - 1, BATCH - 1)
            act.wait_ge(stored, 16 * tiles_before(len(PHASES)))

        @block.vector
        def _(dve):
            def rest_x(ph, b, j):
                n = (ph * BATCH + b) * KC + j
                dve.wait_ge(x_rounded, n + 1)
                nc.vector.tensor_tensor(x_lo[:, j % XSPLIT], x_raw[:, j // XGROUP % XRAW, j % XGROUP],
                                        x_hi[:, j % XSPLIT].bitcast(F32), ALU.subtract
                                        ).then_inc(x_ready, 1)

            def add_identity(ph, k):
                tiles = PHASES[ph]
                n = ph * KC + k
                if k in tiles:
                    at = w_raw[:, n % WRAW, (k - tiles[0]) * P:(k - tiles[0] + 1) * P]
                    dve.wait_ge(w_landed[n % WRAW], 16 * (n // WRAW + 1))
                    nc.vector.tensor_tensor(at, at, ident[:], ALU.add).then_inc(w_diag, 1)

            def rest_w(ph, k):
                n, width = ph * KC + k, len(PHASES[ph]) * P
                dve.wait_ge(w_rounded, n + 1)
                nc.vector.tensor_tensor(w_lo[:, k, 0:width], w_raw[:, n % WRAW, 0:width],
                                        w_hi[:, k, 0:width].bitcast(F32), ALU.subtract
                                        ).then_inc(w_ready, 1)

            def split_w(ph, k):
                add_identity(ph, k)
                rest_w(ph, k)

            def rest_down(b, k):
                dve.wait_ge(down_rounded, b * KC + k + 1)
                nc.vector.tensor_tensor(
                    down[:, k, 6 * RANK:8 * RANK].rearrange("p (s r) -> p s r", s=2),
                    down_raw[:, :, k],
                    down[:, k, 0:2 * RANK].rearrange("p (s r) -> p s r", s=2).bitcast(F32),
                    ALU.subtract).then_inc(down_ready, 1)

            def split_sb(ph):
                width = len(PHASES[ph]) * P
                dve.wait_ge(b_landed, 16 * BATCH * (ph + 1))
                if ph:
                    dve.wait_ge(rank_w_landed, 16 * N_ROW_DMAS * BATCH * ph)
                nc.vector.tensor_scalar(up[:, SB_HI, 0:width], sb_raw[:, 0:width], scale[:, 0:1],
                                        None, ALU.mult).then_inc(sb_hi_done, 1)
                dve.wait_ge(sb_hi_done, ph + 1)
                nc.vector.scalar_tensor_tensor(
                    out=up[:, SB_LO, 0:width], in0=sb_raw[:, 0:width], scalar=scale[:, 0:1],
                    in1=up[:, SB_HI, 0:width].bitcast(F32), op0=ALU.mult, op1=ALU.subtract
                ).then_inc(sb_ready, 1)

            def split_g(ph):
                half = len(PHASES[ph]) * P // 2
                dve.wait_ge(g_done, ph + 1)
                for h in range(2):
                    nc.vector.tensor_copy(up[:, G_HI, h * half:(h + 1) * half],
                                          g_banks[h][:, 0:half]).then_inc(g_hi_done, 1)
                for h in range(2):
                    dve.wait_ge(g_hi_done, 2 * ph + h + 1)
                    nc.vector.tensor_tensor(up[:, G_LO, h * half:(h + 1) * half], g_banks[h][:, 0:half],
                                            up[:, G_HI, h * half:(h + 1) * half].bitcast(F32),
                                            ALU.subtract).then_inc(up_ready, 1)

            def split_z(b):
                lo = slice(4 * RANK, 6 * RANK)
                zb = z_rows[:, bass.ds(b, 1), :].rearrange("p b n -> p (b n)")
                z_lo = z_rows[lo, bass.ds(b, 1), :].rearrange("p b n -> p (b n)")
                dve.wait_ge(z_done, b + 1)
                nc.vector.tensor_copy(zb, z_bank[:]).then_inc(z_hi_done, 1)
                dve.wait_ge(z_hi_done, b + 1)
                nc.vector.tensor_tensor(z_lo, z_bank[lo, :], z_lo.bitcast(F32), ALU.subtract
                                        ).then_inc(z_ready, 1)

            def split_batch(ph, b, previous_z=None, next_w=False, w_left=False):
                for j in range(KC):
                    rest_x(ph, b, j)
                    if w_left and j < LAG:
                        split_w(ph, KC - LAG + j)
                    if j == 1 and previous_z is not None:
                        split_z(previous_z)
                    if w_left and j == LAG - 1:
                        split_g(ph)
                    if next_w and j >= LAG:
                        split_w(ph + 1, j - LAG)
                    if ph == 0 and j < LAG and not (type(b) is int and b == 0):
                        rest_down(b, KC - LAG + j)
                    if ph == 0 and j >= LAG and not (type(b) is int and b == BATCH - 1):
                        rest_down(b + 1, j - LAG)
                if next_w:
                    split_sb(ph + 1)

            dve.wait_ge(A0_rounded, 1)
            nc.vector.tensor_tensor(as_bkr(A0_lo[:]), gathered_bkr, as_bkr(A0_hi[:].bitcast(F32)),
                                    ALU.subtract).then_inc(A0_ready, 1)
            dve.wait_ge(const_landed, 16 * (3 + BATCH))
            for k in range(KC // 2):
                split_w(0, k)
            dve.wait_ge(a_rounded, 1)
            nc.vector.tensor_tensor(as_bkr(a_lo), gathered_bkr, as_bkr(a_hi.bitcast(F32)),
                                    ALU.subtract).then_inc(a_ready, 1)
            for k in range(KC // 2, KC):
                split_w(0, k)
            for k in range(KC):
                rest_down(0, k)
            split_sb(0)
            dve.wait_ge(c_done, 1)
            nc.vector.tensor_tensor(c_raw[:], c_bank[:, 0:P], mask[:], ALU.mult).then_inc(c_masked, 1)
            dve.wait_ge(c_masked, 1)
            nc.vector.tensor_copy(c_split[:, 0], c_raw[:]).then_inc(c_hi_done, 1)
            dve.wait_ge(c_hi_done, 1)
            nc.vector.tensor_tensor(c_split[:, 1], c_raw[:], c_split[:, 0].bitcast(F32), ALU.subtract
                                    ).then_inc(c_ready, 1)
            split_g(0)

            for ph in range(len(PHASES)):
                last_phase = ph == len(PHASES) - 1
                split_batch(ph, 0, BATCH - 1 if ph == 1 else None, w_left=ph > 0)
                with dve.Fori(1, BATCH if last_phase else BATCH - 1) as b:
                    split_batch(ph, b, b - 1 if ph == 0 else None)
                if not last_phase:
                    split_batch(ph, BATCH - 1, BATCH - 2 if ph == 0 else None, next_w=True)

        @block.tensor
        def _(pe):
            def three(bank, hi, lo, moving_hi, moving_lo, start, stop):
                nc.tensor.matmul(bank, hi, moving_hi, start=start, stop=False)
                nc.tensor.matmul(bank, hi, moving_lo, start=False, stop=False)
                return nc.tensor.matmul(bank, lo, moving_hi, start=False, stop=stop)

            def cross():
                pe.wait_ge(a_ready, 1)
                for k in range(KC):
                    last = three(c_bank[:, 0:P], a_hi[:, k], a_lo[:, k], A0_hi[:, k], A0_lo[:, k],
                                 start=k == 0, stop=k == KC - 1)
                last.then_inc(c_done, 1)

            def g_chunks(ph, chunks):
                half = len(PHASES[ph]) * P // 2
                for k in chunks:
                    pe.wait_ge(w_ready, ph * KC + k + 1)
                    for h in range(2):
                        at = slice(h * half, (h + 1) * half)
                        three(g_banks[h][:, 0:half], A0_hi[:, k], A0_lo[:, k], w_hi[:, k, at],
                              w_lo[:, k, at], start=k == 0, stop=False)

            def g_end(ph):
                half = len(PHASES[ph]) * P // 2
                pe.wait_ge(sb_ready, ph + 1)
                if ph == 0:
                    pe.wait_ge(c_ready, 1)
                for h in range(2):
                    at = slice(h * half, (h + 1) * half)
                    last = three(g_banks[h][:, 0:half], c_split[:, 0], c_split[:, 1],
                                 up[:, SB_HI, at], up[:, SB_LO, at], start=False, stop=True)
                last.then_inc(g_done, 1)

            def batch(ph, b):
                n_tiles = len(PHASES[ph])
                first = ph == 0 and type(b) is int and b == 0
                before = tiles_before(ph) + b * n_tiles

                def rank_side(t):
                    moving = z_rows[:, bass.ds(b, 1), :].rearrange("p b n -> p (b n)")
                    nc.tensor.matmul(banks[t][:], rank_w[:, t * P:(t + 1) * P], moving,
                                     start=False, stop=True).then_inc(tile_done, 1)

                for k in range(KC):
                    slot = k % XSPLIT
                    pe.wait_ge(x_ready, (ph * BATCH + b) * KC + k + 1)
                    if ph == 0:
                        pe.wait_ge(down_ready, b * KC + k + 1)
                        if k == 0 and not first:
                            pe.wait_ge(z_ready, b)
                        nc.tensor.matmul(z_bank[:], down[:, k], x_hi[:, slot],
                                         start=k == 0, stop=False)
                        last = nc.tensor.matmul(z_bank[:], down[:, k], x_lo[:, slot],
                                                start=False, stop=k == KC - 1)
                        if k == KC - 1:
                            last.then_inc(z_done, 1)
                    for t in range(n_tiles):
                        if k == 0 and not first:
                            if type(b) is int and b == 0:
                                emptied = min(t, len(PHASES[ph - 1]) - 1) + 1
                                pe.wait_ge(evacuated, before - len(PHASES[ph - 1]) + emptied)
                            else:
                                pe.wait_ge(evacuated, before - n_tiles + t + 1)
                        at = slice(t * P, (t + 1) * P)
                        last = three(banks[t][:], w_hi[:, k, at], w_lo[:, k, at], x_hi[:, slot],
                                     x_lo[:, slot], start=k == 0, stop=False)
                        if t == n_tiles - 1:
                            last.then_inc(chunk_done, 1)
                        if k == KC - 1 and t == n_tiles - 2:
                            pe.wait_ge(rank_w_landed, 16 * N_ROW_DMAS * (ph * BATCH + b + 1))
                            if ph == 0:
                                pe.wait_ge(z_ready, b + 1)
                            elif ph == 1 and type(b) is int and b == 0:
                                pe.wait_ge(z_ready, BATCH)
                            rank_side(0)
                for t in range(1, n_tiles):
                    rank_side(t)

            pe.wait_ge(A0_ready, 1)
            g_chunks(0, range(0, 3 * KC // 4))
            cross()
            g_chunks(0, range(3 * KC // 4, KC))
            g_end(0)
            for ph in range(len(PHASES)):
                if ph:
                    pe.wait_ge(up_ready, 2 * ph)
                    g_chunks(ph, range(KC))
                    g_end(ph)
                batch(ph, 0)
                with pe.Fori(1, BATCH) as b:
                    batch(ph, b)


def kernel(x, itok_B_4_50, itok_B_1_7, L0_cond_A, L0_cond_B, L1_cond_weight, L1_cond_bias,
           L1_cond_lora_a_weights, L1_cond_lora_b_weights, L1_cond_scaling_factors):
    import numpy as _np
    import concourse.bacc as _bacc
    from concourse import mybir as _mybir
    from concourse.bass_utils import run_bass_kernel_spmd as _run

    def chunked(a):
        n, r, _ = a.shape
        return a.reshape(n, r, KC, P).transpose(0, 3, 2, 1).reshape(n, P, KC * r)

    arrays = {
        "x_t": _np.asarray(x).reshape(BATCH, TOK, KC, P).transpose(0, 3, 2, 1),
        "w_t": _np.asarray(L1_cond_weight).T.reshape(KC, P, DIM),
        "bias_t": _np.asarray(L1_cond_bias).reshape(KC, P).T,
        "A0_in": chunked(_np.asarray(L0_cond_A).transpose(0, 2, 1)),
        "B0_in": chunked(_np.asarray(L0_cond_B)),
        "a1_in": chunked(_np.asarray(L1_cond_lora_a_weights)),
        "b1_in": _np.asarray(L1_cond_lora_b_weights).transpose(0, 2, 1),
        "scale_in": _np.repeat(_np.asarray(L1_cond_scaling_factors), RANK).reshape(-1, RANK, 1),
        "ids0": _np.asarray(itok_B_4_50).reshape(1, BATCH),
        "ids1": _np.asarray(itok_B_1_7).reshape(1, BATCH),
        "eye": _np.eye(P, dtype=_np.float32),
        "same_batch": _np.kron(_np.eye(BATCH), _np.ones((RANK, RANK))).astype(_np.float32),
    }
    arrays = {name: _np.ascontiguousarray(a) for name, a in arrays.items()}
    nc = _bacc.Bacc("TRN2", target_bir_lowering=False, num_devices=1)
    aps = [nc.dram_tensor(name, a.shape, _mybir.dt.from_np(a.dtype), kind="ExternalInput").ap()
           for name, a in arrays.items()]
    out_t = nc.dram_tensor("out_t", (BATCH, P, KC, TOK), F32, kind="ExternalOutput").ap()
    up_parts = nc.dram_tensor("up_parts", (4, BATCH * RANK, DIM), F32, kind="Internal").ap()
    two_adapter_layers(nc, *aps, up_parts, out_t)
    got = _run(nc, [arrays], core_ids=[0]).results[0]["out_t"]
    return got.transpose(0, 3, 2, 1).reshape(BATCH, TOK, DIM)
```

```python
from contextlib import ExitStack

import concourse.bass as bass
from concourse import mybir

P = 128
ALU = mybir.AluOpType
ACT = mybir.ActivationFunctionType
F32 = mybir.dt.float32
F32R = mybir.dt.float32r
I32 = mybir.dt.int32

BATCH = 8
TOK = 512
DIM = 2048
RANK = 16
KC = DIM // P
PHASES = [range(0, 5), range(5, 10), range(10, 16)]
WIDEST = max(len(tiles) for tiles in PHASES)
XGROUP = 2
XGROUPS = KC // XGROUP
XRAW = 2
XSPLIT = 4
WRAW = 3
STAGE = 8
LAG = XSPLIT
W_BEHIND_X = [[1], [2], [3], [], [4], [5, 6], [7, 8], [9, 10], [11, 12], [13, 14], [15]] + 5 * [[]]
G_FROM = 5
G_PER_CHUNK = 2
G_END = G_FROM + KC // G_PER_CHUNK - 1
CROSS_AT = G_FROM + 1
Z_TILES = 4
N_PARTS = 4
G_HI, SB_HI, G_LO, SB_LO = range(N_PARTS)
RANK_ROWS = [G_HI, SB_HI, G_LO, SB_LO, G_HI, SB_HI, G_HI, SB_HI]


def two_adapter_layers(
    nc: bass.Bass,
    x_t: bass.AP,
    w_t: bass.AP,
    bias_t: bass.AP,
    A0_in: bass.AP,
    B0_in: bass.AP,
    a1_in: bass.AP,
    b1_in: bass.AP,
    scale_in: bass.AP,
    ids_in: bass.AP,
    same_batch: bass.AP,
    up_parts: bass.AP,
    out_t: bass.AP,
):
    n_adapters0, n_adapters1 = A0_in.shape[0], b1_in.shape[0]

    with ExitStack() as ctx:
        def sb(name, shape, dt=F32):
            return ctx.enter_context(nc.sbuf_tensor(name, shape, dt))

        def sem(name):
            return ctx.enter_context(nc.semaphore(name))

        w_hi = sb("w_hi", [P, KC, WIDEST * P], F32R)
        w_lo = sb("w_lo", [P, KC, WIDEST * P], F32R)
        w_raw = sb("w_raw", [P, WRAW, WIDEST * P])
        x_raw = sb("x_raw", [P, XRAW, XGROUP, TOK])
        x_hi = sb("x_hi", [P, XSPLIT, TOK], F32R)
        x_lo = sb("x_lo", [P, XSPLIT, TOK], F32R)
        z_rows = sb("z_rows", [P, BATCH, TOK], F32R)
        rank_w = sb("rank_w", [P, WIDEST * P], F32R)
        down_raw = sb("down_raw", [P, 2, KC, RANK])
        down = sb("down", [P, KC, P], F32R)
        A0_hi = sb("A0_hi", [P, KC, P], F32R)
        A0_lo = sb("A0_lo", [P, KC, P], F32R)
        up = sb("up", [P, N_PARTS, WIDEST * P], F32R)
        sb_raw = sb("sb_raw", [P, WIDEST * P])
        stage = sb("stage", [P, STAGE, TOK])
        ident = sb("ident", [P, P])
        mask = sb("mask", [P, P])
        c_raw = sb("c_raw", [P, P])
        c_split = sb("c_split", [P, 2, P], F32R)
        bias_sb = sb("bias_sb", [P, KC])
        scale = sb("scale", [P, 1])
        warm = sb("warm", [P, 2])
        ids = sb("ids", [1, 2, BATCH], I32)

        gathered = stage[:].rearrange("p (w t) n -> p w (t n)", w=2)
        A0_raw, a_raw = (gathered[:, which].rearrange("p (b k r) -> p k b r", b=BATCH, k=KC)
                         for which in range(2))
        z_flat = z_rows[:].rearrange("p b n -> p (b n)")
        a_hi = z_flat[:, 0:KC * P].rearrange("p (k m) -> p k m", k=KC)
        a_lo = z_flat[:, KC * P:2 * KC * P].rearrange("p (k m) -> p k m", k=KC)

        def as_bkr(t):
            return t.rearrange("p k (b r) -> p k b r", b=BATCH)

        banks = [ctx.enter_context(nc.psum_tensor(f"bank{i}", [P, TOK], F32)) for i in range(8)]
        z_bank = banks[5]
        g_banks = banks[6:8]
        c_bank = g_banks[1]

        ids_landed = sem("ids_landed")
        warm_set = sem("warm_set")
        ident_cleared = sem("ident_cleared")
        ident_ready = sem("ident_ready")
        const_landed = sem("const_landed")
        scale_landed = sem("scale_landed")
        A0_landed = sem("A0_landed")
        a_landed = sem("a_landed")
        b_landed = sem("b_landed")
        w_landed = [sem(f"w_landed{i}") for i in range(WRAW)]
        x_landed = [sem(f"x_landed{i}") for i in range(XRAW)]
        x_first_landed = sem("x_first_landed")
        down_landed = sem("down_landed")
        parts_saved = sem("parts_saved")
        rank_w_landed = sem("rank_w_landed")
        stored = sem("stored")
        A0_rounded = sem("A0_rounded")
        A0_ready = sem("A0_ready")
        a_rounded = sem("a_rounded")
        a_ready = sem("a_ready")
        w_diag = sem("w_diag")
        w_rounded = sem("w_rounded")
        w_ready = sem("w_ready")
        x_rounded = sem("x_rounded")
        x_ready = sem("x_ready")
        down_rounded = sem("down_rounded")
        down_ready = sem("down_ready")
        chunk_done = sem("chunk_done")
        c_done = sem("c_done")
        c_masked = sem("c_masked")
        c_hi_done = sem("c_hi_done")
        c_ready = sem("c_ready")
        sb_hi_done = sem("sb_hi_done")
        sb_ready = sem("sb_ready")
        g_done = sem("g_done")
        g_hi_done = sem("g_hi_done")
        up_ready = sem("up_ready")
        z_done = sem("z_done")
        z_hi_done = sem("z_hi_done")
        z_ready = sem("z_ready")
        tile_done = sem("tile_done")
        evacuated = sem("evacuated")

        def tiles_before(ph):
            return BATCH * sum(len(t) for t in PHASES[:ph])

        def very_first(ph, b):
            return ph == 0 and type(b) is int and b == 0

        def last_batch(b):
            return type(b) is int and b == BATCH - 1

        def adapter(engine, layer, b):
            last = (n_adapters0, n_adapters1)[layer] - 1
            return engine.value_load(ids[0:1, layer, bass.ds(b, 1)], min_val=0, max_val=last)

        def fill_first_rank_w(engine, ph):
            tiles = PHASES[ph]
            width = len(tiles) * P

            def fill(parts):
                for group, part in enumerate(RANK_ROWS):
                    if part in parts:
                        engine.dma_start(rank_w[group * RANK:(group + 1) * RANK, 0:width].bitcast(F32),
                                         up[0:RANK, part, 0:width].bitcast(F32)
                                         ).then_inc(rank_w_landed, 16)

            if ph:
                engine.wait_ge(tile_done, tiles_before(ph))
            engine.wait_ge(sb_ready, ph + 1)
            fill((SB_HI, SB_LO))
            engine.wait_ge(up_ready, 2 * (ph + 1))
            fill((G_HI, G_LO))

        block = ctx.enter_context(nc.Block())

        @block.sync
        def _(sp):
            def load_x(ph, b, g):
                n = (ph * BATCH + b) * KC + XGROUP * (g - XRAW)
                if not (very_first(ph, b) and g < XRAW):
                    sp.wait_ge(x_ready, n + XGROUP)
                sp.dma_start(x_raw[:, g % XRAW], x_t[bass.ds(b, 1), :, bass.ts(g, XGROUP), :]
                             .rearrange("b p k n -> (b p) k n")).then_inc(x_landed[g % XRAW], 16)

            def load_w(ph, k):
                tiles = PHASES[ph]
                n = ph * KC + k
                if n >= WRAW:
                    sp.wait_ge(w_ready, n - WRAW + 1)
                sp.dma_start(w_raw[:, n % WRAW, 0:len(tiles) * P],
                             w_t[k, :, tiles[0] * P:(tiles[-1] + 1) * P]
                             ).then_inc(w_landed[n % WRAW], 16)

            def load_down(b):
                sp.dma_start(down_raw[:, 0].rearrange("p k r -> p (k r)"),
                             B0_in[bass.ds(adapter(sp, 0, b), 1)].rearrange("a p m -> (a p) m")
                             ).then_inc(down_landed, 16)
                sp.dma_start(down_raw[:, 1].rearrange("p k r -> p (k r)"),
                             a1_in[bass.ds(adapter(sp, 1, b), 1)].rearrange("a p m -> (a p) m")
                             ).then_inc(down_landed, 16)

            def fill_rank_w(ph, b):
                tiles = PHASES[ph]
                sp.wait_ge(parts_saved, 16 * N_PARTS * (ph + 1))
                sp.wait_ge(tile_done, tiles_before(ph) + b * len(tiles))
                for group, part in enumerate(RANK_ROWS):
                    sp.dma_start(rank_w[group * RANK:(group + 1) * RANK, 0:len(tiles) * P].bitcast(F32),
                                 up_parts[part, bass.ds(b * RANK, RANK),
                                          tiles[0] * P:(tiles[-1] + 1) * P]
                                 ).then_inc(rank_w_landed, 16)

            def load_first_batch():
                load_w(0, 0)
                sp.dma_start(x_raw[:, 0, 0], x_t[0, :, 0, :]).then_inc(x_first_landed, 16)
                sp.dma_start(x_raw[:, 0, 1], x_t[0, :, 1, :]).then_inc(x_landed[0], 16)
                load_w(0, 1)
                sp.wait_ge(ids_landed, 16)
                load_down(0)
                load_w(0, 2)
                load_x(0, 0, 1)
                load_w(0, 3)
                load_x(0, 0, 2)
                load_w(0, 4)
                load_w(0, 5)
                load_w(0, 6)
                load_x(0, 0, 3)
                sp.dma_start(mask[:], same_batch).then_inc(const_landed, 16)
                sp.dma_start(bias_sb[:], bias_t).then_inc(const_landed, 16)
                for k in range(7, 10):
                    load_w(0, k)
                load_x(0, 0, 4)
                for k in range(10, 13):
                    load_w(0, k)
                load_x(0, 0, 5)
                for k in range(13, KC):
                    load_w(0, k)
                load_x(0, 0, 6)
                sp.wait_ge(down_ready, KC)
                load_down(1)
                load_x(0, 0, 7)

            for ph in range(len(PHASES)):
                last_phase = ph == len(PHASES) - 1

                def load_batch(b, next_w=False, w_left=False):
                    for g in range(XGROUPS):
                        if next_w:
                            for k in range(max(0, XGROUP * g - 7), max(0, XGROUP * g - 5)):
                                load_w(ph + 1, k)
                        load_x(ph, b, g)
                        if g == LAG // XGROUP + 1 and ph == 0 and not last_batch(b):
                            sp.wait_ge(down_ready, (b + 1) * KC)
                            load_down(b + 1)
                        if w_left and g == 1:
                            load_w(ph, KC - 1)
                        if g == XGROUPS // 2:
                            if w_left:
                                fill_first_rank_w(sp, ph)
                            else:
                                fill_rank_w(ph, b)

                if ph == 0:
                    load_first_batch()
                else:
                    load_batch(0, w_left=True)
                with sp.Fori(1, BATCH if last_phase else BATCH - 1) as b:
                    load_batch(b)
                if not last_phase:
                    load_batch(BATCH - 1, next_w=True)
                    for k in range(KC - 7, KC - 1):
                        load_w(ph + 1, k)

        @block.scalar
        def _(act):
            def round_x(ph, b, j):
                n = (ph * BATCH + b) * KC + j
                g = j // XGROUP
                groups = (ph * BATCH + b) * (XGROUPS // XRAW) + g // XRAW + 1
                if very_first(ph, b) and j == 0:
                    act.wait_ge(x_first_landed, 16)
                elif j % XGROUP == 0 or very_first(ph, b) and j == 1:
                    act.wait_ge(x_landed[g % XRAW], 16 * groups)
                if not (very_first(ph, b) and j < LAG):
                    act.wait_ge(chunk_done, n - LAG + 1)
                nc.scalar.copy(x_hi[:, j % XSPLIT], x_raw[:, g % XRAW, j % XGROUP]
                               ).then_inc(x_rounded, 1)

            def round_w(ph, k):
                tiles = PHASES[ph]
                n, width = ph * KC + k, len(tiles) * P
                if ph:
                    act.wait_ge(chunk_done, (ph * BATCH - 1) * KC + k + 1)
                act.wait_ge(w_landed[n % WRAW], 16 * (n // WRAW + 1))
                if k in tiles:
                    act.wait_ge(w_diag, k + 1)
                nc.scalar.copy(w_hi[:, k, 0:width], w_raw[:, n % WRAW, 0:width]
                               ).then_inc(w_rounded, 1)

            def round_down(b, k):
                if k == 0:
                    act.wait_ge(down_landed, 32 * (b + 1))
                if not very_first(0, b):
                    act.wait_ge(chunk_done, (b - 1) * KC + k + 1)
                nc.scalar.copy(down[:, k, 0:6 * RANK].rearrange("p (g s r) -> p g s r", g=3, s=2),
                               down_raw[:, :, k].unsqueeze(1).to_broadcast([P, 3, 2, RANK])
                               ).then_inc(down_rounded, 1)

            def results(ph, b):
                tiles = PHASES[ph]
                before = tiles_before(ph) + b * len(tiles)
                if not very_first(ph, b):
                    act.wait_ge(stored, 16 * before)

                def store(t):
                    act.wait_ge(evacuated, before + t + 1)
                    act.dma_start(out_t[bass.ds(b, 1), :, tiles[t], :].rearrange("b p n -> (b p) n"),
                                  stage[:, t]).then_inc(stored, 16)

                for t, tile in enumerate(tiles):
                    act.wait_ge(tile_done, before + t + 1)
                    nc.scalar.activation(stage[:, t], banks[t][:], ACT.Identity,
                                         bias=bias_sb[:, tile:tile + 1]).then_inc(evacuated, 1)
                    if t:
                        store(t - 1)
                store(len(tiles) - 1)

            def round_batch(ph, b, previous, next_w=False, w_left=False):
                for j in range(KC):
                    round_x(ph, b, j)
                    if w_left and j < LAG - 1:
                        round_w(ph, KC - LAG + j)
                    if j == LAG - 2:
                        results(*previous)
                    if w_left and j == LAG - 1:
                        round_w(ph, KC - 1)
                    if next_w and j >= LAG:
                        round_w(ph + 1, j - LAG)
                    if ph == 0 and j < LAG:
                        round_down(b, KC - LAG + j)
                    if ph == 0 and j >= LAG and not last_batch(b):
                        round_down(b + 1, j - LAG)

            def round_first_batch():
                act.wait_ge(warm_set, 1)
                nc.scalar.copy(warm[:, 1:2], warm[:, 0:1])
                round_w(0, 0)
                for j in range(KC):
                    round_x(0, 0, j)
                    if j < LAG:
                        for k in range(KC // LAG * j, KC // LAG * (j + 1)):
                            round_down(0, k)
                    for k in W_BEHIND_X[j]:
                        round_w(0, k)
                    if j == LAG - 1:
                        act.wait_ge(A0_landed, 16 * BATCH)
                        nc.scalar.copy(as_bkr(A0_hi[:]), A0_raw).then_inc(A0_rounded, 1)
                    if j == LAG + 1:
                        act.wait_ge(a_landed, 16 * BATCH)
                        nc.scalar.copy(as_bkr(a_hi), a_raw).then_inc(a_rounded, 1)
                act.wait_ge(const_landed, 32)
                act.wait_ge(a_ready, 1)
                for k in range(KC - LAG):
                    round_down(1, k)
                fill_first_rank_w(act, 0)

            for ph in range(len(PHASES)):
                last_phase = ph == len(PHASES) - 1
                if ph == 0:
                    round_first_batch()
                else:
                    round_batch(ph, 0, (ph - 1, BATCH - 1), w_left=True)
                with act.Fori(1, BATCH if last_phase else BATCH - 1) as b:
                    round_batch(ph, b, (ph, b - 1))
                if not last_phase:
                    round_batch(ph, BATCH - 1, (ph, BATCH - 2), next_w=True)
            results(len(PHASES) - 1, BATCH - 1)
            act.wait_ge(stored, 16 * tiles_before(len(PHASES)))

        @block.vector
        def _(dve):
            def rest_x(ph, b, j):
                n = (ph * BATCH + b) * KC + j
                dve.wait_ge(x_rounded, n + 1)
                nc.vector.tensor_tensor(x_lo[:, j % XSPLIT], x_raw[:, j // XGROUP % XRAW, j % XGROUP],
                                        x_hi[:, j % XSPLIT].bitcast(F32), ALU.subtract
                                        ).then_inc(x_ready, 1)

            def add_identity(ph, k):
                tiles = PHASES[ph]
                n = ph * KC + k
                if k in tiles:
                    at = w_raw[:, n % WRAW, (k - tiles[0]) * P:(k - tiles[0] + 1) * P]
                    dve.wait_ge(w_landed[n % WRAW], 16 * (n // WRAW + 1))
                    nc.vector.tensor_tensor(at, at, ident[:], ALU.add).then_inc(w_diag, 1)

            def rest_w(ph, k):
                n, width = ph * KC + k, len(PHASES[ph]) * P
                dve.wait_ge(w_rounded, n + 1)
                nc.vector.tensor_tensor(w_lo[:, k, 0:width], w_raw[:, n % WRAW, 0:width],
                                        w_hi[:, k, 0:width].bitcast(F32), ALU.subtract
                                        ).then_inc(w_ready, 1)

            def split_w(ph, k):
                add_identity(ph, k)
                rest_w(ph, k)

            def rest_down(b, k):
                dve.wait_ge(down_rounded, b * KC + k + 1)
                nc.vector.tensor_tensor(
                    down[:, k, 6 * RANK:8 * RANK].rearrange("p (s r) -> p s r", s=2),
                    down_raw[:, :, k],
                    down[:, k, 0:2 * RANK].rearrange("p (s r) -> p s r", s=2).bitcast(F32),
                    ALU.subtract).then_inc(down_ready, 1)

            def split_sb(ph):
                width = len(PHASES[ph]) * P
                dve.wait_ge(scale_landed, 16 * BATCH)
                dve.wait_ge(b_landed, 16 * BATCH * (ph + 1))
                if ph:
                    dve.wait_ge(rank_w_landed, 16 * len(RANK_ROWS) * BATCH * ph)
                nc.vector.tensor_scalar(up[:, SB_HI, 0:width], sb_raw[:, 0:width], scale[:, 0:1],
                                        None, ALU.mult).then_inc(sb_hi_done, 1)
                dve.wait_ge(sb_hi_done, ph + 1)
                nc.vector.scalar_tensor_tensor(
                    out=up[:, SB_LO, 0:width], in0=sb_raw[:, 0:width], scalar=scale[:, 0:1],
                    in1=up[:, SB_HI, 0:width].bitcast(F32), op0=ALU.mult, op1=ALU.subtract
                ).then_inc(sb_ready, 1)

            def split_g(ph):
                half = len(PHASES[ph]) * P // 2
                dve.wait_ge(g_done, ph + 1)
                for h in range(2):
                    nc.vector.tensor_copy(up[:, G_HI, h * half:(h + 1) * half],
                                          g_banks[h][:, 0:half]).then_inc(g_hi_done, 1)
                for h in range(2):
                    dve.wait_ge(g_hi_done, 2 * ph + h + 1)
                    nc.vector.tensor_tensor(up[:, G_LO, h * half:(h + 1) * half], g_banks[h][:, 0:half],
                                            up[:, G_HI, h * half:(h + 1) * half].bitcast(F32),
                                            ALU.subtract).then_inc(up_ready, 1)

            def split_z(b):
                lo = slice(4 * RANK, 6 * RANK)
                zb = z_rows[:, bass.ds(b, 1), :].rearrange("p b n -> p (b n)")
                z_lo = z_rows[lo, bass.ds(b, 1), :].rearrange("p b n -> p (b n)")
                dve.wait_ge(z_done, b + 1)
                nc.vector.tensor_copy(zb, z_bank[:]).then_inc(z_hi_done, 1)
                dve.wait_ge(z_hi_done, b + 1)
                nc.vector.tensor_tensor(z_lo, z_bank[lo, :], z_lo.bitcast(F32), ALU.subtract
                                        ).then_inc(z_ready, 1)

            def split_batch(ph, b, previous_z=None, next_w=False, w_left=False):
                for j in range(KC):
                    rest_x(ph, b, j)
                    if w_left and j < LAG:
                        split_w(ph, KC - LAG + j)
                    if j == 1 and previous_z is not None:
                        split_z(previous_z)
                    if w_left and j == LAG - 1:
                        split_g(ph)
                    if next_w and j >= LAG:
                        split_w(ph + 1, j - LAG)
                    if ph == 0 and j < LAG:
                        rest_down(b, KC - LAG + j)
                    if ph == 0 and j >= LAG and not last_batch(b):
                        rest_down(b + 1, j - LAG)
                if next_w:
                    split_sb(ph + 1)

            def split_c():
                dve.wait_ge(const_landed, 32)
                dve.wait_ge(c_done, 1)
                nc.vector.tensor_tensor(c_raw[:], c_bank[:, 0:P], mask[:], ALU.mult
                                        ).then_inc(c_masked, 1)
                dve.wait_ge(c_masked, 1)
                nc.vector.tensor_copy(c_split[:, 0], c_raw[:]).then_inc(c_hi_done, 1)
                dve.wait_ge(c_hi_done, 1)
                nc.vector.tensor_tensor(c_split[:, 1], c_raw[:], c_split[:, 0].bitcast(F32),
                                        ALU.subtract).then_inc(c_ready, 1)

            def split_first_batch():
                dve.wait_ge(ident_ready, 1)
                split_w(0, 0)
                for j in range(KC):
                    rest_x(0, 0, j)
                    if j < LAG:
                        for k in range(KC // LAG * j, KC // LAG * (j + 1)):
                            rest_down(0, k)
                    for k in W_BEHIND_X[j]:
                        split_w(0, k)
                    if j == CROSS_AT + LAG - 1:
                        split_c()
                    if j == CROSS_AT + LAG:
                        split_sb(0)
                split_g(0)
                for k in range(KC - LAG):
                    rest_down(1, k)

            for ph in range(len(PHASES)):
                last_phase = ph == len(PHASES) - 1
                if ph == 0:
                    split_first_batch()
                else:
                    split_batch(ph, 0, BATCH - 1 if ph == 1 else None, w_left=True)
                with dve.Fori(1, BATCH if last_phase else BATCH - 1) as b:
                    split_batch(ph, b, b - 1 if ph == 0 else None)
                if not last_phase:
                    split_batch(ph, BATCH - 1, BATCH - 2 if ph == 0 else None, next_w=True)

        @block.gpsimd
        def _(pool):
            def gather(which, layer, source, landed):
                for b in range(BATCH):
                    pool.dma_start(gathered[:, which, bass.ts(b, KC * RANK)],
                                   source[bass.ds(adapter(pool, layer, b), 1)]
                                   .rearrange("a p m -> (a p) m")
                                 ).then_inc(landed, 16)

            def load_b(ph):
                tiles = PHASES[ph]
                if ph:
                    pool.wait_ge(sb_ready, ph)
                for b in range(BATCH):
                    pool.dma_start(sb_raw[b * RANK:(b + 1) * RANK, 0:len(tiles) * P],
                                 b1_in[bass.ds(adapter(pool, 1, b), 1), :,
                                       tiles[0] * P:(tiles[-1] + 1) * P].rearrange("a r o -> (a r) o")).then_inc(b_landed, 16)

            def save_parts(ph):
                tiles = PHASES[ph]
                pool.wait_ge(up_ready, 2 * (ph + 1))
                for part in range(N_PARTS):
                    pool.dma_start(up_parts[part, :, tiles[0] * P:(tiles[-1] + 1) * P],
                                   up[:, part, 0:len(tiles) * P].bitcast(F32)
                                   ).then_inc(parts_saved, 16)

            pool.dma_start(ids[:], ids_in).then_inc(ids_landed, 16)
            nc.gpsimd.memset(warm[:], 0.0).then_inc(warm_set, 1)
            nc.gpsimd.memset(ident[:], 0.0).then_inc(ident_cleared, 1)
            pool.wait_ge(ident_cleared, 1)
            nc.gpsimd.affine_select(out=ident[:], in_=ident[:], compare_op=ALU.not_equal, fill=1.0,
                                    base=0, pattern=[[-1, P]], channel_multiplier=1
                                    ).then_inc(ident_ready, 1)
            pool.wait_ge(ids_landed, 16)
            gather(0, 0, A0_in, A0_landed)
            gather(1, 1, a1_in, a_landed)
            pool.wait_ge(A0_rounded, 1)
            nc.gpsimd.tensor_tensor(as_bkr(A0_lo[:]), A0_raw, as_bkr(A0_hi[:].bitcast(F32)),
                                    ALU.subtract).then_inc(A0_ready, 1)
            pool.wait_ge(a_rounded, 1)
            nc.gpsimd.tensor_tensor(as_bkr(a_lo), a_raw, as_bkr(a_hi.bitcast(F32)),
                                    ALU.subtract).then_inc(a_ready, 1)
            for b in range(BATCH):
                pool.dma_start(scale[bass.ts(b, RANK), :],
                             scale_in[bass.ds(adapter(pool, 1, b), 1)].rearrange("a r c -> (a r) c")
                             ).then_inc(scale_landed, 16)
            load_b(0)
            save_parts(0)
            for ph in range(1, len(PHASES)):
                load_b(ph)
                save_parts(ph)

        @block.tensor
        def _(pe):
            def three(bank, hi, lo, moving_hi, moving_lo, start, stop):
                nc.tensor.matmul(bank, hi, moving_hi, start=start, stop=False)
                nc.tensor.matmul(bank, hi, moving_lo, start=False, stop=False)
                return nc.tensor.matmul(bank, lo, moving_hi, start=False, stop=stop)

            def cross():
                pe.wait_ge(a_ready, 1)
                for k in range(KC):
                    last = three(c_bank[:, 0:P], a_hi[:, k], a_lo[:, k], A0_hi[:, k], A0_lo[:, k],
                                 start=k == 0, stop=k == KC - 1)
                last.then_inc(c_done, 1)

            def g_half(ph, h, chunks):
                half = len(PHASES[ph]) * P // 2
                at = slice(h * half, (h + 1) * half)
                for k in chunks:
                    pe.wait_ge(w_ready, ph * KC + k + 1)
                    three(g_banks[h][:, 0:half], A0_hi[:, k], A0_lo[:, k], w_hi[:, k, at],
                          w_lo[:, k, at], start=k == 0, stop=False)

            def g_end(ph):
                half = len(PHASES[ph]) * P // 2
                pe.wait_ge(sb_ready, ph + 1)
                if ph == 0:
                    pe.wait_ge(c_ready, 1)
                for h in range(2):
                    at = slice(h * half, (h + 1) * half)
                    last = three(g_banks[h][:, 0:half], c_split[:, 0], c_split[:, 1],
                                 up[:, SB_HI, at], up[:, SB_LO, at], start=False, stop=True)
                last.then_inc(g_done, 1)

            def batch(ph, b):
                n_tiles = len(PHASES[ph])
                first = very_first(ph, b)
                before = tiles_before(ph) + b * n_tiles
                behind = Z_TILES - 1 if ph == 0 else 0

                def rank_side(t):
                    moving = z_rows[:, bass.ds(b, 1), :].rearrange("p b n -> p (b n)")
                    nc.tensor.matmul(banks[t][:], rank_w[:, t * P:(t + 1) * P], moving,
                                     start=False, stop=True).then_inc(tile_done, 1)

                def z_part(k):
                    slot = k % XSPLIT
                    pe.wait_ge(down_ready, b * KC + k + 1)
                    if k == 0 and not first:
                        pe.wait_ge(z_ready, b)
                    nc.tensor.matmul(z_bank[:], down[:, k], x_hi[:, slot], start=k == 0, stop=False)
                    last = nc.tensor.matmul(z_bank[:], down[:, k], x_lo[:, slot],
                                            start=False, stop=k == KC - 1)
                    if k == KC - 1:
                        last.then_inc(z_done, 1)
                    return last

                for k in range(KC):
                    slot = k % XSPLIT
                    if first:
                        pe.wait_ge(w_ready, k + 1)
                    pe.wait_ge(x_ready, (ph * BATCH + b) * KC + k + 1)
                    if ph == 0 and not (first and k == 0):
                        z_part(k)
                    for t in range(n_tiles):
                        if k == 0 and not first:
                            n_previous = len(PHASES[ph - 1]) if type(b) is int else n_tiles
                            pe.wait_ge(evacuated, before - n_previous + min(t + 1, n_previous))
                        at = slice(t * P, (t + 1) * P)
                        last = three(banks[t][:], w_hi[:, k, at], w_lo[:, k, at], x_hi[:, slot],
                                     x_lo[:, slot], start=k == 0, stop=False)
                        if t == n_tiles - 1:
                            if first and k == 0:
                                last = z_part(k)
                            last.then_inc(chunk_done, 1)
                        if k == KC - 1 and t == behind:
                            pe.wait_ge(rank_w_landed, 16 * len(RANK_ROWS) * (ph * BATCH + b + 1))
                            pe.wait_ge(z_ready, b + 1 if ph == 0 else BATCH)
                        if k == KC - 1 and t >= behind:
                            rank_side(t - behind)
                    if first and G_FROM <= k <= G_END:
                        at = G_PER_CHUNK * (k - G_FROM)
                        if k == G_FROM:
                            pe.wait_ge(A0_ready, 1)
                        g_half(0, 0, range(at, at + G_PER_CHUNK))
                        if k == CROSS_AT:
                            cross()
                        if k <= CROSS_AT:
                            continue
                        if k == CROSS_AT + 1:
                            pe.wait_ge(c_masked, 1)
                            at = 0
                        g_half(0, 1, range(at, G_PER_CHUNK * (k - G_FROM + 1)))
                    if first and k == G_END:
                        g_end(0)
                for t in range(n_tiles - behind, n_tiles):
                    rank_side(t)

            for ph in range(len(PHASES)):
                if ph:
                    pe.wait_ge(up_ready, 2 * ph)
                    for k in range(KC):
                        for h in range(2):
                            g_half(ph, h, [k])
                    g_end(ph)
                batch(ph, 0)
                with pe.Fori(1, BATCH) as b:
                    batch(ph, b)


def kernel(x, itok_B_4_50, itok_B_1_7, L0_cond_A, L0_cond_B, L1_cond_weight, L1_cond_bias,
           L1_cond_lora_a_weights, L1_cond_lora_b_weights, L1_cond_scaling_factors):
    import numpy as _np
    import concourse.bacc as _bacc
    from concourse import mybir as _mybir
    from concourse.bass_utils import run_bass_kernel_spmd as _run

    def chunked(a):
        n, r, _ = a.shape
        return a.reshape(n, r, KC, P).transpose(0, 3, 2, 1).reshape(n, P, KC * r)

    arrays = {
        "x_t": _np.asarray(x).reshape(BATCH, TOK, KC, P).transpose(0, 3, 2, 1),
        "w_t": _np.asarray(L1_cond_weight).T.reshape(KC, P, DIM),
        "bias_t": _np.asarray(L1_cond_bias).reshape(KC, P).T,
        "A0_in": chunked(_np.asarray(L0_cond_A).transpose(0, 2, 1)),
        "B0_in": chunked(_np.asarray(L0_cond_B)),
        "a1_in": chunked(_np.asarray(L1_cond_lora_a_weights)),
        "b1_in": _np.asarray(L1_cond_lora_b_weights).transpose(0, 2, 1),
        "scale_in": _np.repeat(_np.asarray(L1_cond_scaling_factors), RANK).reshape(-1, RANK, 1),
        "ids_in": _np.stack([itok_B_4_50, itok_B_1_7]).reshape(1, 2, BATCH),
        "same_batch": _np.kron(_np.eye(BATCH), _np.ones((RANK, RANK))).astype(_np.float32),
    }
    arrays = {name: _np.ascontiguousarray(a) for name, a in arrays.items()}
    nc = _bacc.Bacc("TRN2", target_bir_lowering=False, num_devices=1)
    aps = [nc.dram_tensor(name, a.shape, _mybir.dt.from_np(a.dtype), kind="ExternalInput").ap()
           for name, a in arrays.items()]
    out_t = nc.dram_tensor("out_t", (BATCH, P, KC, TOK), F32, kind="ExternalOutput").ap()
    up_parts = nc.dram_tensor("up_parts", (N_PARTS, BATCH * RANK, DIM), F32, kind="Internal").ap()
    two_adapter_layers(nc, *aps, up_parts, out_t)
    got = _run(nc, [arrays], core_ids=[0]).results[0]["out_t"]
    return got.transpose(0, 3, 2, 1).reshape(BATCH, TOK, DIM)
```
